# Optimizing a Trainium2 kernel written in Bass

```python
import numpy as np
import jax
import jax.numpy as jnp

def _softmax(x, axis=-1):
    return jax.nn.softmax(x, axis=axis)

def _gelu(x):
    return jax.nn.gelu(x, approximate=True)

def _silu(x):
    return jax.nn.silu(x)

def _sigmoid(x):
    return jax.nn.sigmoid(x)

def _layernorm(x, axis=-1, eps=1e-05):
    m = jnp.mean(x, axis=axis, keepdims=True)
    v = jnp.var(x, axis=axis, keepdims=True)
    return (x - m) / jnp.sqrt(v + eps)

def _scatter_add(tgt, idx, src, axis=0):
    return tgt.at[idx].add(src)

def _segment_sum(src, seg, n):
    return jax.ops.segment_sum(src, seg, n)
kernel_name = 'mk_gnn_ffn_d1_gnn_r8_34032d'

def setup_inputs(seed: int=0):
    np.random.seed(seed)
    _w = jnp.asarray

    def _rec_inputs():
        import jax
        import jax.numpy as jnp
        _gk = jax.random.key(seed)
        x = -8.776e-05 + 1 * jax.random.normal(jax.random.fold_in(_gk, 1), (2500, 256), jnp.float32)
        src = jax.random.randint(jax.random.fold_in(_gk, 2), (80000,), 0, 2500, jnp.int32)
        dst = jnp.minimum((2500 * jax.random.uniform(jax.random.fold_in(_gk, 3), (80000,)) ** 2.0).astype(jnp.int32), 19999)
        _o = jnp.argsort(dst, stable=True)
        src = src[_o]
        dst = dst[_o]
        edge_weight = jax.random.uniform(jax.random.fold_in(_gk, 12), (80000,), jnp.float32, 0.0, 0.999998)
        return (x, src, dst, edge_weight)
    x, src, dst, edge_weight = _rec_inputs()

    def _L0_gnn_setup():
        import jax, jax.numpy as jnp
        import numpy as np
        N = 2500
        E = 40000
        D_IN = 256
        D_OUT = 256
        BN_EPS = 1e-05

        def _batchnorm(h, gamma, beta):
            mean = jnp.mean(h, axis=0)
            var = jnp.var(h, axis=0)
            return (h - mean) * jax.lax.rsqrt(var + BN_EPS) * gamma + beta
        key = jax.random.key(seed)
        ks = jax.random.split(key, 10)
        x = jax.random.normal(ks[0], (N, D_IN), dtype=jnp.float32)
        edge_index = jax.random.randint(ks[1], (2, E), 0, N, dtype=jnp.int64)
        edge_weight = jax.random.uniform(ks[2], (E,), dtype=jnp.float32)
        s1 = 1.0 / np.sqrt(D_IN)
        s2 = 1.0 / np.sqrt(D_OUT)
        W1 = jax.random.uniform(ks[3], (D_IN, D_OUT), minval=-s1, maxval=s1, dtype=jnp.float32)
        b1 = jax.random.uniform(ks[4], (D_OUT,), minval=-s1, maxval=s1, dtype=jnp.float32)
        g1 = jnp.ones((D_OUT,), jnp.float32)
        be1 = jnp.zeros((D_OUT,), jnp.float32)
        W2 = jax.random.uniform(ks[5], (D_OUT, D_OUT), minval=-s2, maxval=s2, dtype=jnp.float32)
        b2 = jax.random.uniform(ks[6], (D_OUT,), minval=-s2, maxval=s2, dtype=jnp.float32)
        g2 = jnp.ones((D_OUT,), jnp.float32)
        be2 = jnp.zeros((D_OUT,), jnp.float32)
        eps = jnp.zeros((1,), jnp.float32)
        return {'x': x, 'edge_index': edge_index, 'edge_weight': edge_weight, 'W1': W1, 'b1': b1, 'g1': g1, 'be1': be1, 'W2': W2, 'b2': b2, 'g2': g2, 'be2': be2, 'eps': eps}
    _L0_gnn_all = _L0_gnn_setup()
    _L0_gnn_in = {k: v for k, v in _L0_gnn_all.items() if k in ('W1', 'b1', 'g1', 'be1', 'W2', 'b2', 'g2', 'be2', 'eps')}
    del _L0_gnn_all

    def _L0_ffn_setup():
        import jax, jax.numpy as jnp
        import numpy as np
        E = 8
        K = 2
        D = 256
        H = 512
        DOUT = 256
        EPS = 1e-05
        key = jax.random.key(seed)
        ks = jax.random.split(key, 9)
        s = 0.02
        return {'x': jax.random.normal(ks[0], (4, 1024, D), jnp.float32), 'gamma': 1.0 + 0.05 * jax.random.normal(ks[1], (D,), jnp.float32), 'beta': 0.05 * jax.random.normal(ks[2], (D,), jnp.float32), 'Wr': 0.01 * jax.random.normal(ks[3], (D, E), jnp.float32), 'br': jnp.zeros((E,), jnp.float32), 'W1': s * jax.random.normal(ks[4], (E, D, H), jnp.float32), 'b1': s * jax.random.normal(ks[5], (E, H), jnp.float32), 'W2': s * jax.random.normal(ks[6], (E, H, DOUT), jnp.float32), 'b2': s * jax.random.normal(ks[7], (E, DOUT), jnp.float32)}
    _L0_ffn_all = _L0_ffn_setup()
    _L0_ffn_in = {k: v for k, v in _L0_ffn_all.items() if k in ('gamma', 'beta', 'Wr', 'br', 'W1', 'b1', 'W2', 'b2')}
    del _L0_ffn_all
    return {'x': x, 'src': src, 'dst': dst, 'edge_weight': edge_weight, 'L0_gnn_W1': _L0_gnn_in['W1'], 'L0_gnn_b1': _L0_gnn_in['b1'], 'L0_gnn_g1': _L0_gnn_in['g1'], 'L0_gnn_be1': _L0_gnn_in['be1'], 'L0_gnn_W2': _L0_gnn_in['W2'], 'L0_gnn_b2': _L0_gnn_in['b2'], 'L0_gnn_g2': _L0_gnn_in['g2'], 'L0_gnn_be2': _L0_gnn_in['be2'], 'L0_gnn_eps': _L0_gnn_in['eps'], 'L0_ffn_gamma': _L0_ffn_in['gamma'], 'L0_ffn_beta': _L0_ffn_in['beta'], 'L0_ffn_Wr': _L0_ffn_in['Wr'], 'L0_ffn_br': _L0_ffn_in['br'], 'L0_ffn_W1': _L0_ffn_in['W1'], 'L0_ffn_b1': _L0_ffn_in['b1'], 'L0_ffn_W2': _L0_ffn_in['W2'], 'L0_ffn_b2': _L0_ffn_in['b2']}

def reference(x, src, dst, edge_weight, L0_gnn_W1, L0_gnn_b1, L0_gnn_g1, L0_gnn_be1, L0_gnn_W2, L0_gnn_b2, L0_gnn_g2, L0_gnn_be2, L0_gnn_eps, L0_ffn_gamma, L0_ffn_beta, L0_ffn_Wr, L0_ffn_br, L0_ffn_W1, L0_ffn_b1, L0_ffn_W2, L0_ffn_b2):
    import jax
    import jax.numpy as jnp

    def _L0_gnn_ref(x, edge_index, edge_weight, W1, b1, g1, be1, W2, b2, g2, be2, eps):
        import jax, jax.numpy as jnp
        import numpy as np
        N = 2500
        E = 40000
        D_IN = 256
        D_OUT = 256
        BN_EPS = 1e-05

        def _batchnorm(h, gamma, beta):
            mean = jnp.mean(h, axis=0)
            var = jnp.var(h, axis=0)
            return (h - mean) * jax.lax.rsqrt(var + BN_EPS) * gamma + beta
        src = edge_index[0]
        dst = edge_index[1]
        msg = edge_weight[:, None] * x[src]
        agg = jax.ops.segment_sum(msg, dst, num_segments=N)
        out = agg + (1.0 + eps[0]) * x
        h = out @ W1 + b1
        h = _batchnorm(h, g1, be1)
        h = h @ W2 + b2
        h = _batchnorm(h, g2, be2)
        return h

    def _L0_ffn_ref(x, gamma, beta, Wr, br, W1, b1, W2, b2):
        import jax, jax.numpy as jnp
        import numpy as np
        E = 8
        K = 2
        D = 256
        H = 512
        DOUT = 256
        EPS = 1e-05
        mu = jnp.mean(x, axis=-1, keepdims=True)
        var = jnp.mean(jnp.square(x - mu), axis=-1, keepdims=True)
        xn = (x - mu) * jax.lax.rsqrt(var + EPS) * gamma + beta
        logits = jnp.einsum('bsd,de->bse', xn, Wr) + br
        top_vals, top_idx = jax.lax.top_k(logits, K)
        w = jax.nn.softmax(top_vals, axis=-1)
        w_full = jnp.einsum('bsk,bske->bse', w, jax.nn.one_hot(top_idx, E, dtype=w.dtype))
        y = jnp.zeros(x.shape[:-1] + (DOUT,), x.dtype)
        for e in range(E):
            h = jax.nn.gelu(jnp.einsum('bsd,dh->bsh', xn, W1[e]) + b1[e], approximate=False)
            y_e = jnp.einsum('bsh,hd->bsd', h, W2[e]) + b2[e]
            y = y + y_e * w_full[..., e, None]
        return y
    edge_index = jnp.stack([src, dst])
    x = x + _L0_gnn_ref(_layernorm(x, axis=-1), edge_index, edge_weight, L0_gnn_W1, L0_gnn_b1, L0_gnn_g1, L0_gnn_be1, L0_gnn_W2, L0_gnn_b2, L0_gnn_g2, L0_gnn_be2, L0_gnn_eps)
    x = x + _L0_ffn_ref(_layernorm(x, axis=-1)[None], L0_ffn_gamma, L0_ffn_beta, L0_ffn_Wr, L0_ffn_br, L0_ffn_W1, L0_ffn_b1, L0_ffn_W2, L0_ffn_b2)[0]
    return x

_drawn_inputs = setup_inputs


def setup_inputs(seed=0):
    import zlib

    import numpy as np

    out = dict(_drawn_inputs(seed))
    spreads = {'L0_gnn_g1': (1.0, 0.2),
     'L0_gnn_be1': (0.0, 0.8),
     'L0_gnn_g2': (1.0, 0.2),
     'L0_gnn_be2': (0.0, 0.1),
     'L0_ffn_br': (0.0, 0.1)}
    factors = {'L0_gnn_b1': 8.0,
     'L0_gnn_b2': 8.0,
     'L0_ffn_gamma': 8.0,
     'L0_ffn_beta': 6.881,
     'L0_ffn_b1': 8.0,
     'L0_ffn_b2': 6.026}
    for name, (base, spread) in spreads.items():
        noise = np.random.default_rng([zlib.crc32(name.encode()), seed]).standard_normal(out[name].shape)
        drawn = base * np.exp(spread * noise) if base else spread * noise
        out[name] = jnp.asarray(drawn.astype(out[name].dtype))
    for name, factor in factors.items():
        out[name] = (out[name] * factor).astype(out[name].dtype)
    return out
```

```python
from contextlib import ExitStack

import concourse.bass as bass
from concourse import mybir

F32 = mybir.dt.float32
I32 = mybir.dt.int32
BF16 = mybir.dt.bfloat16
ALU = mybir.AluOpType
ACT = mybir.ActivationFunctionType
AX = mybir.AxisListType

P = 128
D = 256
KD = D // P
N = 2500
NP = 125
NT = N // NP
GT = 4
NG = NT // GT
CH = GT * NP
EDGES = 80000
EJ = 5
EG = EDGES // (EJ * P)
RING = 5
WIN = 128
NW = -(-N // WIN)
NE = 8
H = 512
KH = H // P
MAX_TILES = (2 * N + NE * (P - 1)) // P
NS = MAX_TILES + 1
ROW = D + 4
TOK, WT0, WT1, EX0 = D, D + 1, D + 2, D + 3
EPS = 1e-5
BIG = 3.0e38

T_LO, T_CNT_W, T_BASE = 0, 128, 256
T_CNT, T_FIRST, T_ALL = 0, NE, 2 * NE


class Chain:

    def __init__(self, eng, sem):
        self.eng, self.sem, self.n = eng, sem, 0

    def add(self, ins):
        self.n += 1
        ins.then_inc(self.sem, 1)

    def wait(self):
        self.eng.wait_ge(self.sem, self.n)

    def step(self, ins):
        self.add(ins)
        self.wait()


def build(nc, x, src, dst, edge_weight, W1, b1, g1, be1, W2, b2, g2, be2, eps,
          gamma, beta, Wr, br, EW1, Eb1, EW2, Eb2, out):
    xn_dram = nc.dram_tensor("xn_dram", (N, D), F32, kind="Internal").ap()
    slots_dram = nc.dram_tensor("slots_dram", (NS * P, ROW), F32, kind="Internal").ap()
    sum_dram = nc.dram_tensor("sum_dram", (N + P, D), F32, kind="Internal").ap()

    with ExitStack() as ctx:
        def sb(name, shape, dt=F32):
            return ctx.enter_context(nc.sbuf_tensor(name, shape, dt))

        def sem(name):
            return ctx.enter_context(nc.semaphore(name))

        psum = ctx.enter_context(nc.psum_tensor("psum", [P, 8, 512], F32))

        x_sb = sb("x_sb", [NP, NT, D])
        z_sb = sb("z_sb", [NP, NT, ROW])
        agg = sb("agg", [P, KD, NW * WIN])
        hid = sb("hid", [P, KD, N])
        src_i = sb("src_i", [EG, EJ * P], I32)
        dst_i = sb("dst_i", [EG, EJ * P], I32)
        w_r = sb("w_r", [EG, EJ * P])
        src_f = sb("src_f", [EG, EJ * P])
        dst_f = sb("dst_f", [EG, EJ * P])
        win_i = sb("win_i", [EG, EJ * P], I32)
        bounds = sb("bounds", [EG, 3])
        src_t = sb("src_t", [P, EG, EJ])
        dst_t = sb("dst_t", [P, EG, EJ])
        w_t = sb("w_t", [P, EG, EJ])
        win_row = sb("win_row", [1, 512], I32)
        idx = sb("idx", [P, RING, EJ], I32)
        ring = sb("ring", [P, RING, EJ, D])
        onehot = sb("onehot", [P, EJ, WIN])
        iota_f = sb("iota_f", [P, NW * WIN])
        pid = sb("pid", [P, 1])
        ident = sb("ident", [P, P])
        tri = sb("tri", [P, P])
        tri_b = sb("tri_b", [P, P], BF16)
        ones_b = sb("ones_b", [P, P], BF16)
        rev = sb("rev", [P, NE])
        thr = sb("thr", [P, NT])
        ones8 = sb("ones8", [P, NE])
        pad = sb("pad", [P, ROW])
        W1_sb = sb("W1_sb", [P, KD, D])
        W2_sb = sb("W2_sb", [P, KD, D])
        Wr_sb = sb("Wr_sb", [P, KD, NE])
        br_sb = sb("br_sb", [P, NE])
        eps_sb = sb("eps_sb", [P, 1])
        vec_rows = sb("vec_rows", [16, P])
        vec = sb("vec", [P, 16])
        st = sb("st", [P, NT, 6])
        mv = sb("mv", [P, NT, 2])
        rs = sb("rs", [P, NT])
        bst = sb("bst", [P, KD, NG, 6])
        bmv = sb("bmv", [P, KD, 2])
        bsc = sb("bsc", [P, KD])
        bsh = sb("bsh", [P, KD])
        zn = sb("zn", [P, 2, KD, NP])
        lg = sb("lg", [NP, NT, NE])
        lg2 = sb("lg2", [NP, NT, NE])
        cand = sb("cand", [NP, NT, NE])
        oh0 = sb("oh0", [NP, NT, NE])
        oh1 = sb("oh1", [NP, NT, NE])
        picked = sb("picked", [NP, NT + 1, NE], BF16)
        top = sb("top", [NP, 4, NT])
        gap = sb("gap", [NP, 3, NT])
        pos = sb("pos", [NP, NT, NE])
        cnt = sb("cnt", [NP, NE])
        cmpt = sb("cmpt", [NP, NE, NT])
        tiles_e = sb("tiles_e", [NP, NE])
        last_e = sb("last_e", [NP, NE])
        first_e = sb("first_e", [NP, NE])
        slot_i = sb("slot_i", [NP, 2, NT], I32)
        slot_f = sb("slot_f", [NP, 2, NT])
        ex_row = sb("ex_row", [1, 2 * NE + 1], I32)
        w1e = sb("w1e", [P, 2, KD, H])
        w2e = sb("w2e", [P, 2, KH, D])
        b1e = sb("b1e", [P, 2, KH])
        b2e = sb("b2e", [P, 2, D])
        zs = sb("zs", [P, ROW])
        xT = sb("xT", [P, KD, P])
        hT = sb("hT", [P, KH, P])
        meta_next = sb("meta_next", [P, 4])
        wdiff = sb("wdiff", [P, 1])
        wsel = sb("wsel", [P, 1])
        wcur = sb("wcur", [P, 1])
        tcur = sb("tcur", [P, 1])
        tok_i = sb("tok_i", [P, 1], I32)
        y_b = sb("y_b", [P, D])
        y_w = sb("y_w", [P, D])

        s_edges = sem("s_edges")
        s_xin = [sem(f"s_xin{g}") for g in range(NG)]
        s_vecs = sem("s_vecs")
        s_weights = sem("s_weights")
        s_iota = sem("s_iota")
        s_dve = sem("s_dve")
        s_consts = sem("s_consts")
        s_padrow = sem("s_padrow")
        s_padded = sem("s_padded")
        s_ef = sem("s_ef")
        s_bounds = sem("s_bounds")
        s_edgeT = sem("s_edgeT")
        s_rows = sem("s_rows")
        s_vecT = sem("s_vecT")
        s_tables = sem("s_tables")
        s_rcp = sem("s_rcp")
        s_root = sem("s_root")
        s_xn = sem("s_xn")
        s_xn_stored = sem("s_xn_stored")
        s_xnT = sem("s_xnT")
        s_agg0 = sem("s_agg0")
        s_idx = sem("s_idx")
        s_ring = [sem(f"s_ring{j}") for j in range(RING)]
        s_onehot = sem("s_onehot")
        s_summed = sem("s_summed")
        s_agg = sem("s_agg")
        s_mm = [sem(f"s_mm{i}") for i in range(2)]
        s_biased = [sem(f"s_biased{i}") for i in range(2)]
        s_normed = [sem(f"s_normed{i}") for i in range(2)]
        s_backT = sem("s_backT")
        s_x2 = sem("s_x2")
        s_x2_stored = sem("s_x2_stored")
        s_z = sem("s_z")
        s_zT = sem("s_zT")
        s_zn = sem("s_zn")
        s_logits = sem("s_logits")
        s_gap = sem("s_gap")
        s_exp = sem("s_exp")
        s_picked = sem("s_picked")
        s_rank = sem("s_rank")
        s_plan = sem("s_plan")
        s_placed = sem("s_placed")
        s_ew = [sem(f"s_ew{p}") for p in range(2)]
        s_zs = sem("s_zs")
        s_zsT = sem("s_zsT")
        s_meta = sem("s_meta")
        s_xT = sem("s_xT")
        s_h = sem("s_h")
        s_gelu = sem("s_gelu")
        s_y = sem("s_y")
        s_wd = sem("s_wd")
        s_ws = sem("s_ws")
        s_wc = sem("s_wc")
        s_yb = sem("s_yb")
        s_dump = sem("s_dump")
        s_freed = sem("s_freed")
        s_yw = sem("s_yw")
        s_added = sem("s_added")
        s_out = sem("s_out")
        s_passed = [sem(f"s_passed_{e}") for e in ("pool", "pe", "act", "dve")]

        def bank(b):
            return psum[:, b, :]

        x_nodes = x.rearrange("(c p) d -> p c d", p=NP)
        xn_nodes = xn_dram.rearrange("(c p) d -> p c d", p=NP)
        sum_nodes = sum_dram[0:N, :].rearrange("(c p) d -> p c d", p=NP)
        VECS = [b1, g1, be1, b2, g2, be2, gamma, beta]
        B1, G1, BE1, B2, G2, BE2, GA, BE = range(8)

        def v(i, k=None):
            return vec[:, 2 * i:2 * i + 2] if k is None else vec[:, 2 * i + k:2 * i + k + 1]

        def group(g):
            return slice(GT * g, GT * (g + 1))

        def node_tiles(c, n):
            return slice(NP * c, NP * (c + n))

        def load_expert(eng, e, p):
            eng.dma_start(w1e[:, p, :, :], EW1[bass.ds(e, 1), :, :].rearrange("e (k p) h -> p (e k) h", p=P)
                          ).then_inc(s_ew[p], 16)
            eng.dma_start(w2e[:, p, :, :], EW2[bass.ds(e, 1), :, :].rearrange("e (k p) d -> p (e k) d", p=P)
                          ).then_inc(s_ew[p], 16)
            with nc.allow_non_contiguous_dma(reason="512 biases, one to a partition and block"):
                eng.dma_start(b1e[:, p, :], Eb1[bass.ds(e, 1), :].rearrange("e (k p) -> p (e k)", p=P)
                              ).then_inc(s_ew[p], 16)
            eng.dma_start(b2e[:, p, :], Eb2[bass.ds(e, 1), :].to_broadcast([P, D])).then_inc(s_ew[p], 16)

        def each_expert(eng, passed, tile, after=None):
            def pair(i, last):
                for p in range(2):
                    e = 2 * i + p
                    n = eng.value_load(ex_row[0:1, bass.ds(e + T_CNT, 1)], min_val=1, max_val=NT)
                    first = eng.value_load(ex_row[0:1, bass.ds(e + T_FIRST, 1)], min_val=0, max_val=MAX_TILES)
                    eng.wait_ge(s_ew[p], i * 64 + 64)
                    eng.sem_inc(passed, 1)
                    with eng.Fori(0, n) as j:
                        tile(e, p, i, first + j)
                    if after is not None and not last:
                        after(e, p, first + n)

            with eng.Fori(0, NE // 2 - 1) as i:
                pair(i, False)
            pair(NE // 2 - 1, True)

        block = ctx.enter_context(nc.Block())

        @block.sync
        def _(sp):
            sp.dma_start(dst_i[:], dst.rearrange("(q e) -> q e", q=EG)).then_inc(s_edges, 16)
            sp.dma_start(src_i[:], src.rearrange("(q e) -> q e", q=EG)).then_inc(s_edges, 16)
            sp.dma_start(w_r[:], edge_weight.rearrange("(q e) -> q e", q=EG)).then_inc(s_edges, 16)
            for g in range(NG):
                sp.dma_start(x_sb[:, GT * g:GT * (g + 1), :], x_nodes[:, GT * g:GT * (g + 1), :]
                             ).then_inc(s_xin[g], 16)
            for i, vv in enumerate(VECS):
                sp.dma_start(vec_rows[2 * i:2 * i + 2, :], vv.rearrange("(k p) -> k p", p=P)
                             ).then_inc(s_vecs, 16)
            sp.dma_start(eps_sb[:], eps.rearrange("(a b) -> a b", a=1).to_broadcast([P, 1])
                         ).then_inc(s_vecs, 16)
            sp.dma_start(W1_sb[:], W1.rearrange("(k p) d -> p k d", p=P)).then_inc(s_weights, 16)
            sp.dma_start(W2_sb[:], W2.rearrange("(k p) d -> p k d", p=P)).then_inc(s_weights, 16)
            sp.dma_start(Wr_sb[:], Wr.rearrange("(k p) e -> p k e", p=P)).then_inc(s_weights, 16)
            sp.dma_start(br_sb[:], br.rearrange("(a b) -> a b", a=1).to_broadcast([P, NE])
                         ).then_inc(s_weights, 16)
            for p in range(2):
                load_expert(sp, p, p)
            sp.wait_ge(s_padrow, 2)
            sp.dma_start(slots_dram.rearrange("(s p) f -> p s f", p=P),
                         pad[:, :].unsqueeze(1).to_broadcast([P, NS, ROW])).then_inc(s_padded, 16)
            sp.dma_start(sum_dram[N:N + P, :], pad[:, 0:D]).then_inc(s_dump, 16)
            for g in range(NG):
                sp.wait_ge(s_x2, 2 * (g + 1))
                sp.dma_start(sum_nodes[:, GT * g:GT * (g + 1), :], x_sb[:, GT * g:GT * (g + 1), :]
                             ).then_inc(s_x2_stored, 16)
            sp.wait_ge(s_plan, 1)
            total = sp.value_load(ex_row[0:1, T_ALL:T_ALL + 1], min_val=NE, max_val=MAX_TILES)
            sp.wait_ge(s_placed, 16 * 2 * NT)
            with sp.Fori(0, total + 1) as q:
                sp.wait_ge(s_zsT, q + 1)
                sp.wait_ge(s_meta, q + 1)
                sp.dma_start(zs[:], slots_dram[bass.ds(q * P, P), :]).then_inc(s_zs, 16)
            sp.wait_ge(s_added, total * 16)
            sp.dma_start(out.rearrange("(a b) d -> a (b d)", a=100),
                         sum_dram[0:N, :].rearrange("(a b) d -> a (b d)", a=100)).then_inc(s_out, 16)
            sp.wait_ge(s_out, 16)

        @block.gpsimd
        def _(pool):
            nc.gpsimd.iota(iota_f[:], pattern=[[1, NW * WIN]], base=0, channel_multiplier=0,
                           allow_small_or_imprecise_dtypes=True).then_inc(s_iota, 1)
            nc.gpsimd.iota(pid[:], pattern=[[0, 1]], base=0, channel_multiplier=1,
                           allow_small_or_imprecise_dtypes=True).then_inc(s_iota, 1)
            nc.gpsimd.iota(pad[:, TOK:TOK + 1], pattern=[[0, 1]], base=N, channel_multiplier=1,
                           allow_small_or_imprecise_dtypes=True).then_inc(s_padrow, 1)
            pool.wait_ge(s_xn_stored, 16 * NG)
            with pool.Fori(0, EG // RING) as i:
                for j in range(RING):
                    pool.wait_ge(s_idx, i * RING + (j + 1))
                    pool.sem_inc(s_passed[0], 1)
                    for t in range(EJ):
                        pool.indirect_dma_start(
                            out=ring[:, j, t, :], out_offset=None, in_=xn_dram,
                            in_offset=bass.IndirectOffsetOnAxis(ap=idx[:, j, t:t + 1], axis=0),
                        ).then_inc(s_ring[j], 16)
            pool.wait_ge(s_plan, 1)
            pool.wait_ge(s_padded, 16)
            for k in range(2):
                for c in range(NT):
                    pool.indirect_dma_start(
                        out=slots_dram, out_offset=bass.IndirectOffsetOnAxis(ap=slot_i[:, k, c:c + 1], axis=0),
                        in_=z_sb[:, c, :], in_offset=None,
                    ).then_inc(s_placed, 16)
            pool.wait_ge(s_dump, 16)
            pool.wait_ge(s_x2_stored, 16 * NG)
            total = pool.value_load(ex_row[0:1, T_ALL:T_ALL + 1], min_val=NE, max_val=MAX_TILES)
            pool.sem_inc(s_freed, 1)
            with pool.Fori(0, total) as q:
                pool.wait_ge(s_yw, q * 2 + 3)
                pool.sem_inc(s_passed[0], 1)
                pool.indirect_dma_start(
                    out=sum_dram, out_offset=bass.IndirectOffsetOnAxis(ap=tok_i[:, 0:1], axis=0),
                    in_=y_w[:], in_offset=None, compute_op=ALU.add,
                ).then_inc(s_added, 16)
                pool.wait_ge(s_added, q * 16 + 16)
                pool.sem_inc(s_freed, 1)

        @block.scalar
        def _(act):
            for g in range(NG):
                act.wait_ge(s_rcp, g + 1)
                nc.scalar.activation(rs[0:NP, group(g)], rs[0:NP, group(g)], ACT.Sqrt).then_inc(s_root, 1)
            for g in range(NG):
                act.wait_ge(s_xn, GT * (g + 1))
                act.dma_start(xn_nodes[:, GT * g:GT * (g + 1), :], z_sb[:, GT * g:GT * (g + 1), 0:D]
                              ).then_inc(s_xn_stored, 16)
            act.wait_ge(s_tables, 1)
            with act.Fori(0, EG // RING) as i:
                for j in range(RING):
                    g = i * RING + j
                    done = act.value_load(win_row[0:1, bass.ds(g + T_BASE, 1)], min_val=0, max_val=EG * NW)
                    act.wait_ge(s_summed, done * EJ + EJ)
                    nc.scalar.copy(idx[:, j, :], src_t[:, bass.ds(g, 1), :].rearrange("p g t -> p (g t)")
                                   ).then_inc(s_idx, 1)
            for i, (into, b) in enumerate(((hid, B1), (agg, B2))):
                for r in range(NG * KD):
                    c, m = divmod(r, KD)
                    act.wait_ge(s_mm[i], r + 1)
                    nc.scalar.activation(into[:, m, CH * c:CH * (c + 1)], bank(2 + r % 4)[:, 0:CH],
                                         ACT.Identity, bias=v(b, m)).then_inc(s_biased[i], 1)
                act.wait_ge(s_rcp, NG + 1 + i)
                nc.scalar.activation(bsc[:], bsc[:], ACT.Sqrt).then_inc(s_root, 1)
            for c in range(NT + GT):
                if c % GT == 0 and c < NT:
                    g = c // GT
                    act.wait_ge(s_rcp, NG + 3 + g)
                    nc.scalar.activation(rs[0:NP, group(g)], rs[0:NP, group(g)], ACT.Sqrt).then_inc(s_root, 1)
                c -= GT
                if c < 0:
                    continue
                act.wait_ge(s_zT, c + 1)
                if c >= 2:
                    act.wait_ge(s_logits, c - 1)
                for k in range(KD):
                    nc.scalar.activation(zn[:, c % 2, k, :], bank(6 + c % 2)[:, P * k:P * k + NP], ACT.Identity,
                                         bias=v(BE, k), scale=v(GA, k)).then_inc(s_zn, 1)
            act.wait_ge(s_gap, 1)
            nc.scalar.activation(gap[:, 1, :], gap[:, 0, :], ACT.Exp).then_inc(s_exp, 1)

            act.sem_inc(s_gelu, KH)
            act.wait_ge(s_plan, 1)

            def tile(e, p, i, q):
                for m in range(KH):
                    act.wait_ge(s_h, q * KH + (m + 2))
                    act.wait_ge(s_y, q * KH + (m + 1))
                    nc.scalar.activation(hT[:, m, :], bank(2 + m)[:, 0:P], ACT.Gelu,
                                         bias=b1e[:, p, m:m + 1]).then_inc(s_gelu, 1)

            def after(e, p, q):
                act.wait_ge(s_y, q * KH + KH)
                act.wait_ge(s_yb, q + 1)
                act.wait_ge(s_gelu, q * KH + KH)
                load_expert(act, e + 2, p)

            each_expert(act, s_passed[2], tile, after)

        @block.vector
        def _(dve):
            ch = Chain(dve, s_dve)
            V = nc.vector
            ch.add(V.memset(pad[:, 0:TOK], 0.0))
            ch.add(V.memset(pad[:, WT0:ROW], 0.0))
            ch.add(V.memset(agg[:, :, N:NW * WIN], 0.0))
            ch.add(V.memset(ones_b[:], 1.0))
            ch.add(V.memset(ones8[:], 1.0))
            ch.add(V.memset(picked[:, NT, :], 0.0))
            ch.add(V.memset(win_row[:, T_BASE:T_BASE + RING - 1], 0))
            ch.wait()
            dve.wait_ge(s_iota, 2)
            ch.add(V.tensor_scalar(ident[:], iota_f[:, 0:P], pid[:, 0:1], None, ALU.is_equal))
            ch.add(V.tensor_scalar(tri[:], iota_f[:, 0:P], pid[:, 0:1], None, ALU.is_gt))
            ch.add(V.tensor_scalar(tri_b[:], iota_f[:, 0:P], pid[:, 0:1], None, ALU.is_gt))
            ch.add(V.tensor_scalar(rev[:], iota_f[:, 0:NE], -1.0, float(NE), ALU.mult, ALU.add))
            ch.add(V.tensor_scalar(thr[:], iota_f[:, 0:NT], float(P), None, ALU.mult))
            ch.wait()
            dve.sem_inc(s_consts, 1)
            dve.sem_inc(s_padrow, 1)

            dve.wait_ge(s_edges, 48)
            V.tensor_copy(dst_f[:], dst_i[:]).then_inc(s_ef, 1)
            V.tensor_copy(src_f[:], src_i[:]).then_inc(s_ef, 1)
            ch.step(V.tensor_scalar(win_i[:], dst_i[:], 7, None, ALU.arith_shift_right))
            ch.add(V.tensor_reduce(bounds[:, 0:1], win_i[:], AX.X, ALU.min))
            ch.step(V.tensor_reduce(bounds[:, 1:2], win_i[:], AX.X, ALU.max))
            ch.step(V.tensor_scalar(bounds[:, 1:2], bounds[:, 1:2], 1.0, None, ALU.add))
            V.tensor_tensor(bounds[:, 2:3], bounds[:, 1:2], bounds[:, 0:1], ALU.subtract).then_inc(s_bounds, 1)
            dve.wait_ge(s_vecT, 1)
            ch.add(V.tensor_copy(vec[:], bank(7)[:, 0:16]))
            for a, t in enumerate((src_t, dst_t, w_t)):
                dve.wait_ge(s_edgeT, a + 1)
                ch.add(V.tensor_copy(t[:, :, 0:4].rearrange("p q j -> p j q"),
                                     bank(a).rearrange("p (j q) -> p j q", j=4)[:, :, 0:EG]))
            dve.wait_ge(s_edgeT, 4)
            for a, t in enumerate((src_t, dst_t, w_t)):
                ch.add(V.tensor_copy(t[:, :, 4], bank(3)[:, P * a:P * a + EG]))
            dve.wait_ge(s_rows, 1)
            ch.add(V.tensor_copy(win_row[:, T_LO:T_LO + EG], psum[0:1, 4, 0:EG]))
            ch.add(V.tensor_copy(win_row[:, T_CNT_W:T_CNT_W + EG], psum[0:1, 4, 128:128 + EG]))
            ch.step(V.tensor_copy(win_row[:, T_BASE + RING - 1:T_BASE + RING + EG], psum[0:1, 4, 256:256 + EG + 1]))
            dve.sem_inc(s_tables, 1)

            def row_stats(g, scale, shift):
                cs = range(GT * g, GT * (g + 1))
                for c in cs:
                    ch.add(V.bn_stats(st[0:NP, c, :], x_sb[:, c, :]))
                ch.wait()
                for c in cs:
                    ch.add(V.bn_aggr(mv[0:NP, c, :], st[0:NP, c, :]))
                ch.wait()
                ch.step(V.tensor_scalar(rs[0:NP, group(g)], mv[0:NP, group(g), 1], scale, shift,
                                        ALU.mult, ALU.add))
                V.reciprocal(rs[0:NP, group(g)], rs[0:NP, group(g)]).then_inc(s_rcp, 1)

            def row_norm(g, roots, done):
                dve.wait_ge(s_root, roots)
                for c in range(GT * g, GT * (g + 1)):
                    V.tensor_scalar(z_sb[:, c, 0:D], x_sb[:, c, :], mv[0:NP, c, 0:1], rs[0:NP, c:c + 1],
                                    ALU.subtract, ALU.mult).then_inc(done, 1)

            for g in range(NG + 1):
                if g < NG:
                    dve.wait_ge(s_xin[g], 16)
                    row_stats(g, 1.0, EPS)
                if g:
                    row_norm(g - 1, g, s_xn)
            dve.wait_ge(s_vecs, 16 * 9)
            ch.step(V.tensor_scalar(eps_sb[:], eps_sb[:], 1.0, None, ALU.add))
            for u in range(NT // 2):
                dve.wait_ge(s_xnT, u + 1)
                V.tensor_scalar(agg[:, :, node_tiles(2 * u, 2)].rearrange("p k (c n) -> p c k n", c=2),
                                bank(5 + u % 2).rearrange("p (c k n) -> p c k n", c=2, k=KD)[:, :, :, 0:NP],
                                eps_sb[:, 0:1], None, ALU.mult).then_inc(s_agg0, 1)
            dve.wait_ge(s_agg0, NT // 2)

            dve.sem_inc(s_agg, 1)
            with dve.Fori(0, EG // RING) as i:
                for j in range(RING):
                    g = i * RING + j
                    lo = dve.value_load(win_row[0:1, bass.ds(g + T_LO, 1)], min_val=0, max_val=NW - 1)
                    n_win = dve.value_load(win_row[0:1, bass.ds(g + T_CNT_W, 1)], min_val=1, max_val=NW)
                    base = dve.value_load(win_row[0:1, bass.ds(g + T_BASE + RING - 1, 1)],
                                          min_val=0, max_val=EG * NW)
                    with dve.Fori(0, n_win) as j_win:
                        q = base + j_win
                        n = nc.s_assert_within(
                            lo + j_win, 0, NW - 1,
                            skip_runtime_bounds_check_because="the group's last window is below NW")
                        for t in range(EJ):
                            dve.wait_ge(s_summed, q * EJ + (t + 1))
                            V.tensor_scalar(onehot[:, t, :], iota_f[:, bass.ds(n * WIN, WIN)],
                                            dst_t[:, bass.ds(g, 1), t], w_t[:, bass.ds(g, 1), t],
                                            ALU.is_equal, ALU.mult).then_inc(s_onehot, 1)
                        dve.wait_ge(s_summed, q * EJ + 2 * EJ)
                        dve.wait_ge(s_agg, q + 1)
                        V.tensor_tensor(agg[:, :, bass.ds(n * WIN, WIN)], agg[:, :, bass.ds(n * WIN, WIN)],
                                        psum[:, 0:2, 0:WIN], ALU.add).then_inc(s_agg, 1)

            for i, (h, ga, be) in enumerate(((hid, G1, BE1), (agg, G2, BE2))):
                for r in range(NG * KD):
                    c, m = divmod(r, KD)
                    dve.wait_ge(s_biased[i], r + 1)
                    ch.add(V.bn_stats(bst[:, m, c, :], h[:, m, CH * c:CH * (c + 1)]))
                ch.wait()
                for m in range(KD):
                    ch.add(V.bn_aggr(bmv[:, m, :], bst[:, m, :, :]))
                ch.wait()
                ch.step(V.tensor_scalar(bsc[:], bmv[:, :, 1], EPS, None, ALU.add))
                V.reciprocal(bsc[:], bsc[:]).then_inc(s_rcp, 1)
                dve.wait_ge(s_root, NG + 1 + i)
                ch.step(V.tensor_tensor(bsc[:], bsc[:], v(ga), ALU.mult))
                ch.step(V.tensor_tensor(bsh[:], bmv[:, :, 0], bsc[:], ALU.mult))
                ch.step(V.tensor_tensor(bsh[:], v(be), bsh[:], ALU.subtract))
                for r in range(NG * KD):
                    c, m = divmod(r, KD)
                    V.tensor_scalar(h[:, m, CH * c:CH * (c + 1)], h[:, m, CH * c:CH * (c + 1)],
                                    bsc[:, m:m + 1], bsh[:, m:m + 1], ALU.mult, ALU.add
                                    ).then_inc(s_normed[i], 1)

            for g in range(NG + 1):
                if g < NG:
                    for u in (2 * g, 2 * g + 1):
                        dve.wait_ge(s_backT, u + 1)
                        V.tensor_tensor(x_sb[:, 2 * u:2 * u + 2, :], x_sb[:, 2 * u:2 * u + 2, :],
                                        bank(2 + u % 4)[0:NP, :].rearrange("p (c d) -> p c d", c=2),
                                        ALU.add).then_inc(s_x2, 1)
                    dve.wait_ge(s_x2, 2 * g + 2)
                    row_stats(g, 1.0 + EPS, EPS * EPS)
                if g:
                    row_norm(g - 1, NG + 2 + g, s_z)

            e_bc = [NP, NT, NE]
            rev_bc = rev[0:NP, :].unsqueeze(1).to_broadcast(e_bc)
            dve.wait_ge(s_logits, NT)
            ch.step(V.tensor_tensor(lg[:], psum[0:NP, 0, 0:NT * NE].rearrange("p (c e) -> p c e", e=NE),
                                    br_sb[0:NP, :].unsqueeze(1).to_broadcast(e_bc), ALU.add))
            for k, (l, oh) in enumerate(((lg, oh0), (lg2, oh1))):
                best, which = top[:, k, :], top[:, 2 + k, :]
                ch.step(V.tensor_reduce(best, l[:], AX.X, ALU.max))
                ch.step(V.tensor_tensor(cand[:], l[:], best.unsqueeze(2).to_broadcast(e_bc), ALU.is_equal))
                ch.step(V.tensor_tensor(cand[:], cand[:], rev_bc, ALU.mult))
                ch.step(V.tensor_reduce(which, cand[:], AX.X, ALU.max))
                ch.step(V.tensor_tensor(oh[:], which.unsqueeze(2).to_broadcast(e_bc), rev_bc, ALU.is_equal))
                if k == 0:
                    ch.step(V.scalar_tensor_tensor(out=lg2[:], in0=oh0[:], scalar=-BIG, in1=lg[:],
                                                   op0=ALU.mult, op1=ALU.add))
            V.tensor_tensor(picked[:, 0:NT, :], oh0[:], oh1[:], ALU.add).then_inc(s_picked, 1)
            V.tensor_tensor(gap[:, 0, :], top[:, 1, :], top[:, 0, :], ALU.subtract).then_inc(s_gap, 1)
            dve.wait_ge(s_exp, 1)
            ch.step(V.tensor_scalar(gap[:, 2, :], gap[:, 1, :], 1.0, None, ALU.add))
            ch.step(V.reciprocal(gap[:, 2, :], gap[:, 2, :]))
            ch.add(V.tensor_copy(z_sb[:, :, WT0], gap[:, 2, :]))
            ch.add(V.tensor_tensor(z_sb[:, :, WT1], gap[:, 1, :], gap[:, 2, :], ALU.mult))
            ch.add(V.tensor_scalar(z_sb[:, :, EX0], top[:, 2, :], -1.0, float(NE), ALU.mult, ALU.add))
            ch.add(V.tensor_scalar(z_sb[:, :, TOK], iota_f[0:NP, 0:NT], float(NP), pid[0:NP, 0:1],
                                   ALU.mult, ALU.add))
            dve.wait_ge(s_rank, 1)
            ch.step(V.tensor_copy(cnt[:], psum[0:NP, 1, NT * NE:(NT + 1) * NE]))
            ch.step(V.tensor_tensor(cmpt[:], thr[0:NP, :].unsqueeze(1).to_broadcast([NP, NE, NT]),
                                    cnt[:].unsqueeze(2).to_broadcast([NP, NE, NT]), ALU.is_lt))
            ch.step(V.tensor_reduce(tiles_e[:], cmpt[:], AX.X, ALU.add))
            ch.step(V.tensor_scalar(tiles_e[:], tiles_e[:], 1.0, None, ALU.max))
            ch.step(V.tensor_tensor_scan(last_e[:], ones8[0:NP, :], tiles_e[:], 0.0, ALU.mult, ALU.add))
            ch.step(V.tensor_tensor(first_e[:], last_e[:], tiles_e[:], ALU.subtract))
            ch.add(V.tensor_copy(ex_row[:, T_CNT:T_CNT + NE], tiles_e[0:1, :]))
            ch.add(V.tensor_copy(ex_row[:, T_FIRST:T_FIRST + NE], first_e[0:1, :]))
            ch.step(V.tensor_copy(ex_row[:, T_ALL:T_ALL + 1], last_e[0:1, NE - 1:NE]))
            ch.step(V.tensor_scalar(first_e[:], first_e[:], float(P), None, ALU.mult))
            ch.step(V.tensor_tensor(pos[:], psum[0:NP, 1, 0:NT * NE].rearrange("p (c e) -> p c e", e=NE),
                                    first_e[:].unsqueeze(1).to_broadcast(e_bc), ALU.add))
            ch.add(V.tensor_tensor(cand[:], pos[:], oh0[:], ALU.mult))
            ch.step(V.tensor_tensor(lg2[:], pos[:], oh1[:], ALU.mult))
            ch.add(V.tensor_reduce(slot_f[:, 0, :], cand[:], AX.X, ALU.add))
            ch.step(V.tensor_reduce(slot_f[:, 1, :], lg2[:], AX.X, ALU.add))
            ch.step(V.tensor_copy(slot_i[:], slot_f[:]))
            dve.sem_inc(s_plan, 1)

            def take(q):
                dve.wait_ge(s_zsT, q + 2)
                dve.wait_ge(s_h, q * KH + 1)
                for k in range(KD):
                    V.tensor_scalar(xT[:, k, :], bank(6)[:, P * k:P * (k + 1)], v(GA, k), v(BE, k),
                                    ALU.mult, ALU.add).then_inc(s_xT, 1)
                dve.wait_ge(s_wc, q * 2 + 1)
                V.tensor_copy(meta_next[:], zs[:, TOK:ROW]).then_inc(s_meta, 1)

            def tile(e, p, i, q):
                dve.wait_ge(s_meta, q + 2)
                dve.wait_ge(s_yw, q * 2 + 1)
                V.tensor_tensor(wdiff[:], meta_next[:, 1:2], meta_next[:, 2:3], ALU.subtract).then_inc(s_wd, 1)
                dve.wait_ge(s_wd, q + 1)
                V.scalar_tensor_tensor(out=wsel[:], in0=meta_next[:, 3:4], scalar=iota_f[:, bass.ds(e, 1)],
                                       in1=wdiff[:], op0=ALU.is_equal, op1=ALU.mult).then_inc(s_ws, 1)
                dve.wait_ge(s_ws, q + 1)
                V.tensor_tensor(wcur[:], wsel[:], meta_next[:, 2:3], ALU.add).then_inc(s_wc, 1)
                V.tensor_copy(tcur[:], meta_next[:, 0:1]).then_inc(s_wc, 1)
                take(q + 1)
                dve.wait_ge(s_y, q * KH + 2 * KH)
                dve.wait_ge(s_yw, q * 2 + 1)
                V.tensor_tensor(y_b[:], bank(0)[:, 0:D], b2e[:, p, :], ALU.add).then_inc(s_yb, 1)
                dve.wait_ge(s_freed, q + 1)
                dve.wait_ge(s_yb, q + 2)
                dve.wait_ge(s_wc, q * 2 + 3)
                V.tensor_copy(tok_i[:], tcur[:]).then_inc(s_yw, 1)
                V.tensor_scalar(y_w[:], y_b[:], wcur[:, 0:1], None, ALU.mult).then_inc(s_yw, 1)

            for first in (s_meta, s_wc, s_xT, s_yb, s_yw):
                dve.sem_inc(first, 1)
            take(0)
            each_expert(dve, s_passed[3], tile)

        @block.tensor
        def _(pe):
            T = nc.tensor
            pe.wait_ge(s_consts, 1)
            pe.wait_ge(s_vecs, 16 * 9)
            T.transpose(bank(7)[:, 0:16], vec_rows[:], ident[0:16, 0:16]).then_inc(s_vecT, 1)
            pe.wait_ge(s_ef, 2)
            for a, f in enumerate((src_f, dst_f, w_r)):
                for t in range(4):
                    last = T.transpose(bank(a)[:, P * t:P * t + EG], f[:, P * t:P * (t + 1)],
                                       ident[0:EG, 0:EG])
                last.then_inc(s_edgeT, 1)
            for a, f in enumerate((src_f, dst_f, w_r)):
                last = T.transpose(bank(3)[:, P * a:P * a + EG], f[:, 4 * P:5 * P], ident[0:EG, 0:EG])
            last.then_inc(s_edgeT, 1)
            pe.wait_ge(s_bounds, 1)
            T.matmul(psum[0:1, 4, 0:EG], bounds[:, 0:1], ident[0:EG, 0:EG], start=True, stop=True)
            T.matmul(psum[0:1, 4, 128:128 + EG], bounds[:, 2:3], ident[0:EG, 0:EG], start=True, stop=True)
            T.matmul(psum[0:1, 4, 256:256 + EG + 1], bounds[:, 2:3], tri[0:EG, 0:EG + 1], start=True, stop=True
                     ).then_inc(s_rows, 1)
            for u in range(NT // 2):
                pe.wait_ge(s_xn, 2 * u + 2)
                if u >= 2:
                    pe.wait_ge(s_agg0, u - 1)
                for c in range(2):
                    for k in range(KD):
                        last = T.transpose(bank(5 + u % 2)[:, P * (KD * c + k):P * (KD * c + k) + NP],
                                           z_sb[:, 2 * u + c, P * k:P * (k + 1)], ident[0:NP, 0:NP])
                last.then_inc(s_xnT, 1)
            pe.wait_ge(s_tables, 1)
            pe.sem_inc(s_summed, EJ)
            with pe.Fori(0, EG // RING) as i:
                for j in range(RING):
                    g = i * RING + j
                    n_win = pe.value_load(win_row[0:1, bass.ds(g + T_CNT_W, 1)], min_val=1, max_val=NW)
                    base = pe.value_load(win_row[0:1, bass.ds(g + T_BASE + RING - 1, 1)],
                                         min_val=0, max_val=EG * NW)
                    pe.wait_ge(s_ring[j], i * (16 * EJ) + 16 * EJ)
                    pe.sem_inc(s_passed[1], 1)
                    with pe.Fori(0, n_win) as j_win:
                        q = base + j_win
                        pe.wait_ge(s_agg, q + 1)
                        for t in range(EJ):
                            pe.wait_ge(s_onehot, q * EJ + (t + 1))
                            for k in range(KD):
                                last = T.matmul(bank(k)[:, 0:WIN], ring[:, j, t, P * k:P * (k + 1)],
                                                onehot[:, t, :], start=(t == 0), stop=(t == EJ - 1))
                            last.then_inc(s_summed, 1)

            pe.wait_ge(s_weights, 64)
            pairs = pe.value_load(win_row[0:1, T_BASE + RING - 1 + EG:T_BASE + RING + EG],
                                  min_val=EG, max_val=EG * NW)
            pe.wait_ge(s_agg, pairs + 1)
            for i, (inp, w) in enumerate(((agg, W1_sb), (hid, W2_sb))):
                for r in range(NG * KD):
                    c, m = divmod(r, KD)
                    if i == 1:
                        pe.wait_ge(s_normed[0], KD * (c + 1))
                    if r >= 4:
                        pe.wait_ge(s_biased[i], r - 3)
                    for k in range(KD):
                        last = T.matmul(bank(2 + r % 4)[:, 0:CH], w[:, k, P * m:P * (m + 1)],
                                        inp[:, k, CH * c:CH * (c + 1)], start=(k == 0), stop=(k == KD - 1))
                    last.then_inc(s_mm[i], 1)

            def back(u):
                pe.wait_ge(s_normed[1], KD * (u // 2 + 1))
                if u >= 4:
                    pe.wait_ge(s_x2, u - 3)
                for c in range(2):
                    for k in range(KD):
                        last = T.transpose(bank(2 + u % 4)[0:NP, D * c + P * k:D * c + P * (k + 1)],
                                           agg[:, k, node_tiles(2 * u + c, 1)], ident[:, :])
                last.then_inc(s_backT, 1)

            def turn(c):
                pe.wait_ge(s_z, c + 1)
                if c >= 2:
                    pe.wait_ge(s_zn, KD * (c - 1))
                for k in range(KD):
                    last = T.transpose(bank(6 + c % 2)[:, P * k:P * k + NP], z_sb[:, c, P * k:P * (k + 1)],
                                       ident[0:NP, 0:NP])
                last.then_inc(s_zT, 1)

            def logits(c):
                pe.wait_ge(s_zn, KD * (c + 1))
                for k in range(KD):
                    last = T.matmul(bank(0)[0:NP, NE * c:NE * (c + 1)], zn[:, c % 2, k, :], Wr_sb[:, k, :],
                                    start=(k == 0), stop=(k == KD - 1))
                last.then_inc(s_logits, 1)

            for u in range(4):
                back(u)
            for g in range(NG):
                for c in range(GT * g, GT * (g + 1)):
                    turn(c)
                    if c:
                        logits(c - 1)
                for u in (2 * g + 4, 2 * g + 5):
                    if u < NT // 2:
                        back(u)
            logits(NT - 1)
            pe.wait_ge(s_picked, 1)
            rank = psum[0:NP, 1, 0:(NT + 1) * NE]
            T.matmul(rank, tri_b[0:NP, 0:NP], picked[:].rearrange("p c e -> p (c e)"), start=True, stop=True,
                     skip_group_check=True)
            for c in range(NT):
                last = T.matmul(psum[0:NP, 1, (c + 1) * NE:(NT + 1) * NE], ones_b[0:NP, 0:NP],
                                picked[:, c, :].unsqueeze(1).to_broadcast([NP, NT - c, NE]),
                                start=False, stop=True, skip_group_check=True)
            last.then_inc(s_rank, 1)

            def turn_slots(q):
                pe.wait_ge(s_zs, q * 16 + 16)
                pe.wait_ge(s_xT, q * KD + 1)
                for k in range(KD):
                    last = T.transpose(bank(6)[:, P * k:P * (k + 1)], zs[:, P * k:P * (k + 1)], ident[:, :])
                last.then_inc(s_zsT, 1)

            def tile(e, p, i, q):
                pe.wait_ge(s_xT, q * KD + (KD + 1))
                for m in range(KH):
                    pe.wait_ge(s_gelu, q * KH + (m + 1))
                    for k in range(KD):
                        last = T.matmul(bank(2 + m)[:, 0:P], w1e[:, p, k, P * m:P * (m + 1)], xT[:, k, :],
                                        start=(k == 0), stop=(k == KD - 1))
                    last.then_inc(s_h, 1)
                turn_slots(q + 1)
                pe.wait_ge(s_yb, q + 1)
                for m in range(KH):
                    pe.wait_ge(s_gelu, q * KH + (m + 1 + KH))
                    T.matmul(bank(0)[:, 0:D], hT[:, m, :], w2e[:, p, m, :],
                             start=(m == 0), stop=(m == KH - 1)).then_inc(s_y, 1)

            pe.wait_ge(s_plan, 1)
            pe.sem_inc(s_y, KH)
            pe.sem_inc(s_zsT, 1)
            pe.sem_inc(s_h, 1)
            turn_slots(0)
            each_expert(pe, s_passed[1], tile)


_INS = ['x', 'src', 'dst', 'edge_weight', 'L0_gnn_W1', 'L0_gnn_b1', 'L0_gnn_g1', 'L0_gnn_be1', 'L0_gnn_W2',
        'L0_gnn_b2', 'L0_gnn_g2', 'L0_gnn_be2', 'L0_gnn_eps', 'L0_ffn_gamma', 'L0_ffn_beta', 'L0_ffn_Wr',
        'L0_ffn_br', 'L0_ffn_W1', 'L0_ffn_b1', 'L0_ffn_W2', 'L0_ffn_b2']


def kernel(**inputs):
    import numpy as _np
    import concourse.bacc as _bacc
    from concourse import mybir as _mybir
    from concourse.bass_utils import run_bass_kernel_spmd as _run

    nc = _bacc.Bacc("TRN2", target_bir_lowering=False, num_devices=1)
    arrays, args = {}, []
    for name in _INS:
        a = _np.ascontiguousarray(inputs[name])
        arrays[f"in_{name}_dram"] = a
        args.append(nc.dram_tensor(f"in_{name}_dram", a.shape, _mybir.dt.from_np(a.dtype), kind="ExternalInput").ap())
    args.append(nc.dram_tensor("out_0_dram", (N, D), F32, kind="ExternalOutput").ap())
    build(nc, *args)
    r = _run(nc, [arrays], core_ids=[0])
    return r.results[0]["out_0_dram"]
```
